# Optimizing a Trainium2 kernel written in Bass

```python
import numpy as np
import jax
import jax.numpy as jnp

def _softmax(x, axis=-1):
    return jax.nn.softmax(x, axis=axis)

def _gelu(x):
    return jax.nn.gelu(x, approximate=True)

def _silu(x):
    return jax.nn.silu(x)

def _sigmoid(x):
    return jax.nn.sigmoid(x)

def _layernorm(x, axis=-1, eps=1e-05):
    m = jnp.mean(x, axis=axis, keepdims=True)
    v = jnp.var(x, axis=axis, keepdims=True)
    return (x - m) / jnp.sqrt(v + eps)

def _scatter_add(tgt, idx, src, axis=0):
    return tgt.at[idx].add(src)

def _segment_sum(src, seg, n):
    return jax.ops.segment_sum(src, seg, n)
kernel_name = 'mk_cond_resid_d1_seqx_r4_355262'

def setup_inputs(seed: int=0):
    np.random.seed(seed)
    _w = jnp.asarray

    def _rec_inputs():
        import jax
        import jax.numpy as jnp
        _rk = jax.random.key(seed)
        x = -0.000125 + 0.9999 * jax.random.normal(jax.random.fold_in(_rk, 1), (8, 512, 256), jnp.float32)
        _lenS = 512 - jax.random.randint(jax.random.fold_in(_rk, 7), (8,), 0, max(1, 512 // 4) + 1, jnp.int32)
        _lenS2 = 512 - jax.random.randint(jax.random.fold_in(_rk, 8), (8,), 0, max(1, 512 // 4) + 1, jnp.int32)
        cond_1024 = -0.00493535 + 1.00056 * jax.random.normal(jax.random.fold_in(_rk, 11), (8, 256), jnp.float32)
        return (x, cond_1024)
    x, cond_1024 = _rec_inputs()

    def _L0_cond_setup():
        import jax, jax.numpy as jnp
        import numpy as np
        import math
        N, T, D, H = (64, 128, 256, 256)

        def lstm_forward(x, h0, Wx, Wh, b):
            Hd = h0.shape[1]
            xW = jnp.einsum('ntd,dg->ntg', x, Wx) + b
            c0 = jnp.zeros_like(h0)

            def step(carry, xw_t):
                prev_h, prev_c = carry
                a = xw_t + prev_h @ Wh
                i = jax.nn.sigmoid(a[:, :Hd])
                f = jax.nn.sigmoid(a[:, Hd:2 * Hd])
                o = jax.nn.sigmoid(a[:, 2 * Hd:3 * Hd])
                g = jnp.tanh(a[:, 3 * Hd:])
                next_c = f * prev_c + i * g
                next_h = o * jnp.tanh(next_c)
                return ((next_h, next_c), next_h)
            (_, _), hs = jax.lax.scan(step, (h0, c0), jnp.swapaxes(xW, 0, 1))
            return jnp.swapaxes(hs, 0, 1)
        key = jax.random.key(seed)
        k1, k2, k3, k4 = jax.random.split(key, 4)
        x = jax.random.normal(k1, (N, T, D), dtype=jnp.float32)
        h0 = jax.random.normal(k2, (N, H), dtype=jnp.float32)
        Wx = jax.random.normal(k3, (D, 4 * H), dtype=jnp.float32) / math.sqrt(D)
        Wh = jax.random.normal(k4, (H, 4 * H), dtype=jnp.float32) / math.sqrt(H)
        b = jnp.zeros((4 * H,), dtype=jnp.float32)
        return {'x': x, 'h0': h0, 'Wx': Wx, 'Wh': Wh, 'b': b}
    _L0_cond_all = _L0_cond_setup()
    _L0_cond_in = {k: v for k, v in _L0_cond_all.items() if k in ('Wx', 'Wh', 'b')}
    del _L0_cond_all
    return {'x': x, 'cond_1024': cond_1024, 'L0_cond_Wx': _L0_cond_in['Wx'], 'L0_cond_Wh': _L0_cond_in['Wh'], 'L0_cond_b': _L0_cond_in['b']}

def reference(x, cond_1024, L0_cond_Wx, L0_cond_Wh, L0_cond_b):
    import jax
    import jax.numpy as jnp

    def _L0_cond_ref(x, h0, Wx, Wh, b):
        import jax, jax.numpy as jnp
        import numpy as np
        import math
        N, T, D, H = (64, 128, 256, 256)

        def lstm_forward(x, h0, Wx, Wh, b):
            Hd = h0.shape[1]
            xW = jnp.einsum('ntd,dg->ntg', x, Wx) + b
            c0 = jnp.zeros_like(h0)

            def step(carry, xw_t):
                prev_h, prev_c = carry
                a = xw_t + prev_h @ Wh
                i = jax.nn.sigmoid(a[:, :Hd])
                f = jax.nn.sigmoid(a[:, Hd:2 * Hd])
                o = jax.nn.sigmoid(a[:, 2 * Hd:3 * Hd])
                g = jnp.tanh(a[:, 3 * Hd:])
                next_c = f * prev_c + i * g
                next_h = o * jnp.tanh(next_c)
                return ((next_h, next_c), next_h)
            (_, _), hs = jax.lax.scan(step, (h0, c0), jnp.swapaxes(xW, 0, 1))
            return jnp.swapaxes(hs, 0, 1)
        return lstm_forward(x, h0, Wx, Wh, b)
    x = x + _L0_cond_ref(x, cond_1024, L0_cond_Wx, L0_cond_Wh, L0_cond_b)
    return x

_drawn_inputs = setup_inputs


def setup_inputs(seed=0):
    import zlib

    import numpy as np

    out = dict(_drawn_inputs(seed))
    spreads = {'L0_cond_b': (0.0, 0.1)}
    factors = {}
    for name, (base, spread) in spreads.items():
        noise = np.random.default_rng([zlib.crc32(name.encode()), seed]).standard_normal(out[name].shape)
        drawn = base * np.exp(spread * noise) if base else spread * noise
        out[name] = jnp.asarray(drawn.astype(out[name].dtype))
    for name, factor in factors.items():
        out[name] = (out[name] * factor).astype(out[name].dtype)
    return out
```

```python
import concourse.bass as bass
from concourse import mybir
from contextlib import ExitStack


def lstm_residual(nc, x, h0, Wx, Wh, b, out):
    fp32 = mybir.dt.float32
    bf16 = mybir.dt.bfloat16
    ALU = mybir.AluOpType
    ACT = mybir.ActivationFunctionType

    N, T, D = x.shape
    HID = h0.shape[1]
    P = 128
    KD = D // P
    C = HID // P
    G = 4
    REF_GATE = [3, 1, 0, 2]
    TS = 8
    COLS = TS * N
    HALVES = 2
    TURNS = T // (TS * HALVES)
    STEPS = TS * HALVES

    ctx = ExitStack()
    with ctx:
        def sb(name, shape, dt=fp32):
            return ctx.enter_context(nc.sbuf_tensor(name, shape, dt))

        def ps(name, shape, dt=fp32):
            return ctx.enter_context(nc.psum_tensor(name, shape, dt))

        def sem(name):
            return ctx.enter_context(nc.semaphore(name))

        wx = sb("wx", [P, KD, G * HID])
        wh = sb("wh", [P, C, G * HID])
        bias = sb("bias", [G, HID])
        gate_of_col = sb("gate_of_col", [G, G, COLS])
        ident = sb("ident", [P, P])
        x_rows = [sb(f"x_rows{h}", [KD * COLS, P]) for h in range(HALVES)]
        xT = [sb(f"xT{h}", [P, KD, COLS]) for h in range(HALVES)]
        h0_rows = sb("h0_rows", [N, HID])
        H_init = sb("H_init", [P, C, N])
        H = [sb(f"H{h}", [P, C, TS, N]) for h in range(HALVES)]
        halves = sb("halves", [P, C, COLS])
        h_half = sb("h_half", [P, C, COLS])
        yT = sb("yT", [P, C, COLS])
        y_rows = sb("y_rows", [C * COLS, P])
        X = [[sb(f"X{p}{c}", [P, 1 + G, N]) for c in range(C)] for p in range(2)]
        FI = [sb(f"FI{c}", [P, 2, N]) for c in range(C)]
        tanh_c = [sb(f"tanh_c{c}", [P, N]) for c in range(C)]

        Z = [[ps(f"Z{h}{c}", [P, 512]) for c in range(C)] for h in range(HALVES)]
        xT_ps = ps("xT_ps", [P, 512])
        y_ps = ps("y_ps", [P, 512])

        weights_in = sem("weights_in")
        bias_in = sem("bias_in")
        h0_in = sem("h0_in")
        x_in = [sem(f"x_in{h}") for h in range(HALVES)]
        ident_made = sem("ident_made")
        scaled = sem("scaled")
        h0_T = sem("h0_T")
        h0_copied = sem("h0_copied")
        xT_made = sem("xT_made")
        xT_copied = sem("xT_copied")
        z_started = sem("z_started")
        z_done = [sem(f"z_done{c}") for c in range(C)]
        gates_done = [sem(f"gates_done{c}") for c in range(C)]
        fi_done = [sem(f"fi_done{c}") for c in range(C)]
        S_done = [sem(f"S_done{c}") for c in range(C)]
        tanh_done = [sem(f"tanh_done{c}") for c in range(C)]
        H_done = [sem(f"H_done{c}") for c in range(C)]
        half_done = sem("half_done")
        yT_done = sem("yT_done")
        y_made = sem("y_made")
        y_copied = sem("y_copied")
        y_out = sem("y_out")

        def slot_cols(z, g, s0, s1):
            return z[:, (g * TS + s0) * N:(g * TS + s1) * N]

        def gate_w(w, k, g, c):
            at = REF_GATE[g] * HID + c * P
            return w[:, k, at:at + P]

        block = ctx.enter_context(nc.Block())

        def turns(eng, body):
            body(0, True, False)
            with eng.Fori(1, TURNS - 1) as i:
                body(i, False, False)
            body(TURNS - 1, False, True)

        @block.sync
        def _(sp):
            def load_x(i, half):
                t0 = i * STEPS + half * TS
                for k in range(KD):
                    src = x[:, bass.ds(t0, TS), k * P:(k + 1) * P].rearrange("n t d -> t n d")
                    sp.dma_start(x_rows[half][k * COLS:(k + 1) * COLS, :], src).then_inc(x_in[half], 16)

            def store_y(t0):
                for c in range(C):
                    dst = out[:, bass.ds(t0, TS), c * P:(c + 1) * P].rearrange("n t d -> t n d")
                    sp.dma_start(dst, y_rows[c * COLS:(c + 1) * COLS, :]).then_inc(y_out, 16)

            load_x(0, 0)
            load_x(0, 1)
            sp.dma_start(h0_rows[:, :], h0).then_inc(h0_in, 16)
            for g in range(G):
                sp.dma_start(bias[g:g + 1, :], b[REF_GATE[g] * HID:(REF_GATE[g] + 1) * HID]
                             .rearrange("(a n) -> a n", a=1)).then_inc(bias_in, 16)

            def body(i, first, last):
                for half in range(HALVES):
                    g = i * HALVES + half
                    if not last:
                        sp.wait_ge(xT_made, g + 1)
                        load_x(i + 1, half)
                    if not (first and half == 0):
                        sp.wait_ge(y_copied, g)
                        store_y(i * STEPS + half * TS - TS)
            turns(sp, body)
            sp.wait_ge(y_copied, TURNS * HALVES)
            store_y(T - TS)
            sp.wait_ge(y_out, 16 * C * TURNS * HALVES)

        @block.gpsimd
        def _(pool):
            nc.gpsimd.dma_start(wx[:, :, :], Wx.rearrange("(k p) n -> p k n", p=P)).then_inc(weights_in, 16)
            nc.gpsimd.dma_start(wh[:, :, :], Wh.rearrange("(k p) n -> p k n", p=P)).then_inc(weights_in, 16)
            nc.gpsimd.memset(ident[:, :], 0.0).then_inc(ident_made, 1)
            nc.gpsimd.memset(gate_of_col[:, :, :], 0.0).then_inc(ident_made, 1)
            nc.gpsimd.memset(halves[:, :, :], 0.5).then_inc(ident_made, 1)
            pool.wait_ge(ident_made, 3)
            nc.gpsimd.affine_select(out=ident[:, :], in_=ident[:, :], compare_op=ALU.not_equal, fill=1.0, base=0,
                                    pattern=[[-1, P]], channel_multiplier=1).then_inc(ident_made, 1)
            nc.gpsimd.affine_select(out=gate_of_col[:, :, :], in_=gate_of_col[:, :, :], compare_op=ALU.not_equal,
                                    fill=1.0, base=0, pattern=[[-1, G], [0, COLS]],
                                    channel_multiplier=1).then_inc(ident_made, 1)

            def residual(g, half):
                for c in range(C):
                    pool.wait_ge(H_done[c], (g + 1) * TS)
                pool.wait_ge(xT_copied, g + 1)
                nc.gpsimd.tensor_tensor(h_half[:, :, :], H[half][:, :, :, :].rearrange("p c t n -> p c (t n)"),
                                        halves[:, :, :], ALU.mult).then_inc(half_done, 1)
                pool.wait_ge(half_done, g + 1)
                nc.gpsimd.tensor_tensor(yT[:, :, :], h_half[:, :, :], xT[half][:, :, :], ALU.add).then_inc(yT_done, 1)

            def body(i, first, last):
                for half in range(HALVES):
                    if not (first and half == 0):
                        residual(i * HALVES + half - 1, 1 - half)
            turns(pool, body)
            residual(TURNS * HALVES - 1, 1)

        @block.scalar
        def _(act):
            def copy_xT(g, half, spare):
                act.wait_ge(xT_made, g + 1)
                if spare:
                    act.wait_ge(yT_done, g - 1)
                nc.scalar.activation(xT[half][:, :, :].rearrange("p k c -> p (k c)"), xT_ps[:, 0:KD * COLS],
                                     ACT.Copy).then_inc(xT_copied, 1)

            def copy_y(g):
                act.wait_ge(y_made, g + 1)
                if not (isinstance(g, int) and g == 0):
                    act.wait_ge(y_out, 16 * C * g)
                nc.scalar.activation(y_rows[:, :], y_ps[:, 0:P], ACT.Copy).then_inc(y_copied, 1)

            act.wait_ge(h0_T, 1)
            nc.scalar.activation(H_init[:, :, :].rearrange("p c n -> p (c n)"), y_ps[:, 0:C * N], ACT.Copy,
                                 scale=2.0).then_inc(h0_copied, 1)
            copy_xT(0, 0, False)

            def step(t, half, s):
                par = s % 2
                for c in range(C):
                    act.wait_ge(z_done[c], t + 1)
                    zs = Z[half][c][:, 0:G * COLS].rearrange("p (g t n) -> p g t n", g=G, t=TS)[:, :, s, :]
                    nc.scalar.activation(X[par][c][:, 1:1 + G, :], zs, ACT.Tanh).then_inc(gates_done[c], 1)
                for c in range(C):
                    act.wait_ge(S_done[c], t + 2)
                    nc.scalar.activation(tanh_c[c][:, :], X[1 - par][c][:, 0, :], ACT.Tanh,
                                         scale=0.5).then_inc(tanh_done[c], 1)

            def body(i, first, last):
                for half in range(HALVES):
                    g = i * HALVES + half
                    for s in range(TS):
                        step(i * STEPS + half * TS + s, half, s)
                        if s == 1 and not (last and half == 1):
                            copy_xT(g + 1, 1 - half, not (first and half == 0))
                        if s == 3 and not (first and half == 0):
                            copy_y(g - 1)
            turns(act, body)
            copy_y(TURNS * HALVES - 1)

        @block.vector
        def _(dve):
            for c in range(C):
                nc.vector.memset(X[0][c][:, 0, :], 0.0).then_inc(S_done[c], 1)
            dve.wait_ge(weights_in, 32)
            sig = slice(0, 3 * HID)
            tan = slice(3 * HID, 4 * HID)
            nc.vector.tensor_scalar(wx[:, :, sig], wx[:, :, sig], 0.5, None, ALU.mult).then_inc(scaled, 1)
            nc.vector.tensor_scalar(wh[:, :, sig], wh[:, :, sig], 0.25, None, ALU.mult).then_inc(scaled, 1)
            nc.vector.tensor_scalar(wh[:, :, tan], wh[:, :, tan], 0.5, None, ALU.mult).then_inc(scaled, 1)
            dve.wait_ge(ident_made, 5)
            nc.vector.tensor_scalar(gate_of_col[:, 1:G, :], gate_of_col[:, 1:G, :], 0.5, None,
                                    ALU.mult).then_inc(scaled, 1)

            def step(t, half, s):
                par = s % 2
                for c in range(C):
                    now, nxt = X[par][c], X[1 - par][c]
                    dve.wait_ge(gates_done[c], t + 1)
                    nc.vector.scalar_tensor_tensor(out=FI[c][:, :, :], in0=now[:, 2:4, :], scalar=1.0,
                                                   in1=now[:, 0:2, :], op0=ALU.add, op1=ALU.mult).then_inc(fi_done[c], 1)
                    dve.wait_ge(fi_done[c], t + 1)
                    nc.vector.scalar_tensor_tensor(out=nxt[:, 0, :], in0=FI[c][:, 0, :], scalar=0.5,
                                                   in1=FI[c][:, 1, :], op0=ALU.mult, op1=ALU.add).then_inc(S_done[c], 1)
                for c in range(C):
                    now = X[par][c]
                    dve.wait_ge(tanh_done[c], t + 1)
                    nc.vector.scalar_tensor_tensor(out=H[half][:, c, s, :], in0=now[:, 4, :], scalar=1.0,
                                                   in1=tanh_c[c][:, :], op0=ALU.add, op1=ALU.mult).then_inc(H_done[c], 1)

            def body(i, first, last):
                for half in range(HALVES):
                    if not (first or False):
                        dve.wait_ge(half_done, i * HALVES + half - 1)
                    for s in range(TS):
                        step(i * STEPS + half * TS + s, half, s)
            turns(dve, body)

        @block.tensor
        def _(pe):
            def transpose_x(g, half, i):
                pe.wait_ge(x_in[half], 16 * KD * (i + 1))
                if not (isinstance(g, int) and g == 0):
                    pe.wait_ge(xT_copied, g)
                nc.tensor.transpose(xT_ps[:, 0:P], x_rows[half][:, :], ident[:, :]).then_inc(xT_made, 1)

            def projections(half):
                for c in range(C):
                    z = Z[half][c]

                    def bias_mm(c=c, z=z):
                        return nc.tensor.matmul(z[:, 0:G * COLS], bias[:, c * P:(c + 1) * P],
                                                gate_of_col[:, :, :].rearrange("p g c -> p (g c)"),
                                                start=True, stop=False, skip_group_check=True)
                    yield bias_mm
                for c in range(C):
                    for g in range(G):
                        for k in range(KD):
                            def x_mm(c=c, g=g, k=k):
                                return nc.tensor.matmul(slot_cols(Z[half][c], g, 0, TS), gate_w(wx, k, g, c),
                                                        xT[half][:, k, :], start=False, stop=False,
                                                        skip_group_check=True)
                            yield x_mm

            def transpose_y(g):
                pe.wait_ge(yT_done, g + 1)
                if not (isinstance(g, int) and g == 0):
                    pe.wait_ge(y_copied, g)
                nc.tensor.transpose(y_ps[:, 0:P], yT[:, :, :].rearrange("p c n -> p (c n)"),
                                    ident[:, :]).then_inc(y_made, 1)

            def recur(half, s, k, c, last_k):
                if s == 0:
                    state = H_prev[half](k)
                else:
                    state = H[half][:, k, s - 1, :]
                for g in range(G):
                    mm = nc.tensor.matmul(slot_cols(Z[half][c], g, s, s + 1), gate_w(wh, k, g, c), state,
                                          start=False, stop=True, skip_group_check=True)
                if last_k:
                    mm.then_inc(z_done[c], 1)

            pe.wait_ge(ident_made, 5)
            pe.wait_ge(h0_in, 16)
            for c in range(C):
                mm = nc.tensor.transpose(y_ps[:, c * N:(c + 1) * N], h0_rows[:, c * P:(c + 1) * P], ident[0:N, 0:N])
            mm.then_inc(h0_T, 1)
            transpose_x(0, 0, 0)
            pe.wait_ge(scaled, 4)
            pe.wait_ge(bias_in, 16 * G)
            pe.wait_ge(xT_copied, 1)
            for mm in projections(0):
                mm()

            H_prev = None

            def body(i, first, last):
                nonlocal H_prev
                for half in range(HALVES):
                    g = i * HALVES + half
                    H_prev = {half: (lambda k: H_init[:, k, :]) if first and half == 0 else
                              (lambda k, half=half: H[1 - half][:, k, TS - 1, :])}
                    more = not (last and half == 1)
                    todo = list(projections(1 - half)) if more else []
                    share = -(-len(todo) // (TS - 2))
                    for s in range(TS):
                        t = i * STEPS + half * TS + s
                        start = first and half == 0 and s == 0
                        if start:
                            pe.wait_ge(h0_copied, 1)
                        else:
                            pe.wait_ge(H_done[0], t)
                        recur(half, s, 0, 0, False)
                        if not start:
                            pe.wait_ge(gates_done[1], t)
                        recur(half, s, 0, 1, False)
                        if not start:
                            pe.wait_ge(H_done[1], t)
                        recur(half, s, 1, 0, True)
                        recur(half, s, 1, 1, True)
                        if s == 0 and more:
                            transpose_x(g + 1, 1 - half, i + half)
                        if s == 1 and not (first and half == 0):
                            transpose_y(g - 1)
                        if s >= 2:
                            if s == 2 and more:
                                pe.wait_ge(xT_copied, g + 2)
                            for mm in todo[:share]:
                                mm()
                            todo = todo[share:]

            turns(pe, body)
            transpose_y(TURNS * HALVES - 1)


_INS = ["x", "cond_1024", "L0_cond_Wx", "L0_cond_Wh", "L0_cond_b"]
_OUT = ((8, 512, 256), "float32")


def kernel(**inputs):
    import numpy as _np
    import concourse.bacc as _bacc
    from concourse import mybir as _mybir
    from concourse.bass_utils import run_bass_kernel_spmd as _run

    nc = _bacc.Bacc("TRN2", target_bir_lowering=False, num_devices=1)
    arrays, args = {}, []
    for name in _INS:
        a = _np.ascontiguousarray(inputs[name])
        arrays[f"in_{name}"] = a
        args.append(nc.dram_tensor(f"in_{name}", a.shape, _mybir.dt.from_np(a.dtype), kind="ExternalInput").ap())
    args.append(nc.dram_tensor("out_0", _OUT[0], _mybir.dt.from_np(_np.dtype(_OUT[1])), kind="ExternalOutput").ap())
    lstm_residual(nc, *args)
    r = _run(nc, [arrays], core_ids=[0])
    return r.results[0]["out_0"]
```

```python
import concourse.bass as bass
from concourse import mybir
from contextlib import ExitStack


def lstm_residual(nc, x, h0, Wx, Wh, b, out):
    fp32 = mybir.dt.float32
    bf16 = mybir.dt.bfloat16
    ALU = mybir.AluOpType
    ACT = mybir.ActivationFunctionType
    AX = mybir.AxisListType

    N, T, D = x.shape
    HID = h0.shape[1]
    P = 128
    KD = D // P
    C = HID // P
    G = 4
    REF_GATE = [3, 1, 0, 2]
    PARTS = 3
    TS = 16
    COLS = TS * N
    HALVES = 2
    STEPS = TS * HALVES
    TURNS = T // STEPS
    GROUPS = T // TS
    TILES = C * G
    PIECES = 2
    PS = TS // PIECES
    EARLY = 2

    ctx = ExitStack()
    with ctx:
        def sb(name, shape, dt=fp32):
            return ctx.enter_context(nc.sbuf_tensor(name, shape, dt))

        def ps(name, shape, dt=fp32):
            return ctx.enter_context(nc.psum_tensor(name, shape, dt))

        def sem(name):
            return ctx.enter_context(nc.semaphore(name))

        wx = sb("wx", [P, KD, G * HID])
        wh = sb("wh", [P, C, G * HID])
        wh_rest = sb("wh_rest", [P, C, G * HID])
        wh_part = [sb(f"wh_part{p}", [P, C, G * HID], bf16) for p in range(PARTS)]
        bias_raw = sb("bias_raw", [P, TILES])
        bias = sb("bias", [P, TILES])
        ident = sb("ident", [P, P])
        ident_bf = sb("ident_bf", [P, P], bf16)
        x_rows = [sb(f"x_rows{h}", [COLS, D]) for h in range(HALVES)]
        xT = [sb(f"xT{h}", [P, KD, COLS]) for h in range(HALVES)]
        XZ = [sb(f"XZ{h}", [P, PARTS * TILES * COLS]) for h in range(HALVES)]
        h0_rows = sb("h0_rows", [N, HID])
        H = [sb(f"H{h}", [P, C * PARTS * COLS]) for h in range(HALVES)]
        H0 = sb("H_init", [P, C * PARTS * N])
        halves = sb("halves", [P, C, PS * N])
        h_half = [sb(f"h_half{p}", [P, C, PS * N]) for p in range(PIECES)]
        yT = sb("yT", [P, C, COLS])
        y_rows = sb("y_rows", [COLS, D])
        X = [[sb(f"X{p}{c}", [P, 1 + G, N]) for c in range(C)] for p in range(2)]
        FI = [sb(f"FI{c}", [P, 2, N]) for c in range(C)]
        tanh_c = [sb(f"tanh_c{c}", [P, N]) for c in range(C)]

        Z = [[ps(f"Z{p}{c}", [P, 512]) for c in range(C)] for p in range(2)]
        XP = [ps(f"XP{p}", [P, 512]) for p in range(2)]
        xT_ps = ps("xT_ps", [P, 512])
        y_ps = ps("y_ps", [P, 512])

        wx_in = sem("wx_in")
        wh_in = sem("wh_in")
        bias_in = sem("bias_in")
        h0_in = sem("h0_in")
        x_in = [sem(f"x_in{h}") for h in range(HALVES)]
        consts_made = sem("consts_made")
        ident_bf_made = sem("ident_bf_made")
        bias_made = sem("bias_made")
        wh_split = sem("wh_split")
        h0_T = sem("h0_T")
        h0_copied = sem("h0_copied")
        H0_split = sem("H0_split")
        xT_made = sem("xT_made")
        xT_copied = sem("xT_copied")
        xp_made = sem("xp_made")
        xp_copied = sem("xp_copied")
        xz_rest = sem("xz_rest")
        z_done = [sem(f"z_done{c}") for c in range(C)]
        summed = [sem(f"summed{c}") for c in range(C)]
        gates_done = [sem(f"gates_done{c}") for c in range(C)]
        fi_done = [sem(f"fi_done{c}") for c in range(C)]
        S_done = [sem(f"S_done{c}") for c in range(C)]
        tanh_done = [sem(f"tanh_done{c}") for c in range(C)]
        H_done = [sem(f"H_done{c}") for c in range(C)]
        rest_done = [sem(f"rest_done{c}") for c in range(C)]
        state_done = [sem(f"state_done{c}") for c in range(C)]
        half_done = sem("half_done")
        yT_done = sem("yT_done")
        y_made = sem("y_made")
        y_copied = sem("y_copied")
        y_out = sem("y_out")

        H_val = [t[:, :].rearrange("q (c p t n) -> q c p t n", c=C, p=PARTS, t=TS) for t in H]
        H_up = [t[:, :].bitcast(bf16).rearrange("q (c p t n u) -> q c p t n u", c=C, p=PARTS, t=TS, u=2) for t in H]
        H0_val = H0[:, :].rearrange("q (p c n) -> q p c n", c=C, p=PARTS)
        H0_up = H0[:, :].bitcast(bf16).rearrange("q (p c n u) -> q p c n u", c=C, p=PARTS, u=2)
        XZ_val = [t[:, :].rearrange("q (p j t) -> q p j t", p=PARTS, j=TILES) for t in XZ]
        XZ_up = [t[:, :].bitcast(bf16).rearrange("q (p j t u) -> q p j t u", p=PARTS, j=TILES, u=2) for t in XZ]

        def gate_w(w, k, g, c):
            at = REF_GATE[g] * HID + c * P
            return w[:, k, at:at + P]

        MMS = TILES * KD

        def proj_step(m):
            return 1 + m * 12 // MMS

        block = ctx.enter_context(nc.Block())

        def turns(eng, body):
            body(0, True, False)
            with eng.Fori(1, TURNS - 1) as i:
                body(i, False, False)
            body(TURNS - 1, False, True)

        @block.sync
        def _(sp):
            def load_x(i, half):
                t0 = i * STEPS + half * TS
                src = x[:, bass.ds(t0, TS), :].rearrange("n t d -> t n d")
                sp.dma_start(x_rows[half][:, :], src).then_inc(x_in[half], 16)

            def store_y(t0):
                dst = out[:, bass.ds(t0, TS), :].rearrange("n t d -> t n d")
                sp.dma_start(dst, y_rows[:, :]).then_inc(y_out, 16)

            sp.dma_start(h0_rows[:, :], h0).then_inc(h0_in, 16)
            load_x(0, 0)
            sp.dma_start(wx[:, :, :], Wx.rearrange("(k p) n -> p k n", p=P)).then_inc(wx_in, 16)
            for g in range(G):
                for c in range(C):
                    at = REF_GATE[g] * HID + c * P
                    j = c * G + g
                    sp.dma_start(bias_raw[:, j:j + 1], b[at:at + P].rearrange("(p a) -> p a", a=1)).then_inc(bias_in, 16)
            load_x(0, 1)

            def body(i, first, last):
                for half in range(HALVES):
                    g = i * HALVES + half
                    if not last:
                        sp.wait_ge(xT_made, g + 1)
                        load_x(i + 1, half)
                    if not (first and half == 0):
                        sp.wait_ge(y_copied, g)
                        store_y(i * STEPS + half * TS - TS)
            turns(sp, body)
            sp.wait_ge(y_copied, GROUPS)
            store_y(T - TS)
            sp.wait_ge(y_out, 16 * GROUPS)

        @block.gpsimd
        def _(pool):
            nc.gpsimd.memset(ident[:, :], 0.0).then_inc(consts_made, 1)
            nc.gpsimd.memset(halves[:, :, :], 0.5).then_inc(consts_made, 1)
            pool.wait_ge(consts_made, 2)
            nc.gpsimd.affine_select(out=ident[:, :], in_=ident[:, :], compare_op=ALU.not_equal, fill=1.0, base=0,
                                    pattern=[[-1, P]], channel_multiplier=1).then_inc(consts_made, 1)

            def split_xz(g, half, j0, j1):
                lot = j0 // (j1 - j0)
                lots = TILES // (j1 - j0)
                pool.wait_ge(xp_copied, g * TILES + j1)
                for p in range(1, PARTS):
                    if p > 1:
                        pool.wait_ge(xz_rest, (g * lots + lot) * (PARTS - 1) + p - 1)
                    nc.gpsimd.tensor_tensor(XZ_val[half][:, p, j0:j1, :], XZ_val[half][:, p - 1, j0:j1, :],
                                            XZ_up[half][:, p - 1, j0:j1, :, 1], ALU.subtract).then_inc(xz_rest, 1)

            def residual(g, half, piece):
                done = g * TS + (piece + 1) * PS
                for c in range(C):
                    pool.wait_ge(H_done[c], done)
                if not (isinstance(g, int) and g == 0):
                    pool.wait_ge(y_made, g)
                pool.wait_ge(xT_copied, g + 1)
                s0, s1 = piece * PS, (piece + 1) * PS
                nc.gpsimd.tensor_tensor(h_half[piece][:, :, :], H_val[half][:, :, 0, s0:s1, :].rearrange("q c t n -> q c (t n)"),
                                        halves[:, :, :], ALU.mult).then_inc(half_done, 1)
                pool.wait_ge(half_done, g * PIECES + piece + 1)
                nc.gpsimd.tensor_tensor(yT[:, :, s0 * N:s1 * N], h_half[piece][:, :, :], xT[half][:, :, s0 * N:s1 * N],
                                        ALU.add).then_inc(yT_done, 1)

            for j in range(0, TILES, 2):
                split_xz(0, 0, j, j + 2)

            def body(i, first, last):
                for half in range(HALVES):
                    g = i * HALVES + half
                    more = not (last and half == 1)
                    if not (first and half == 0):
                        residual(g - 1, 1 - half, 1)
                    for j in range(0, TILES // 2, 2):
                        if more:
                            split_xz(g + 1, 1 - half, j, j + 2)
                    residual(g, half, 0)
                    for j in range(TILES // 2, TILES, 2):
                        if more:
                            split_xz(g + 1, 1 - half, j, j + 2)
            turns(pool, body)
            residual(GROUPS - 1, 1, 1)

        @block.scalar
        def _(act):
            act.dma_start(wh[:, :, :], Wh.rearrange("(k p) n -> p k n", p=P)).then_inc(wh_in, 16)

            def copy_xT(g, half):
                act.wait_ge(xT_made, g + 1)
                if not isinstance(g, int) or g >= 2:
                    act.wait_ge(yT_done, (g - 1) * PIECES)
                nc.scalar.activation(xT[half][:, :, :].rearrange("p k c -> p (k c)"), xT_ps[:, 0:KD * COLS],
                                     ACT.Copy).then_inc(xT_copied, 1)

            def copy_xp(g, half, j):
                act.wait_ge(xp_made, g * TILES + j + 1)
                nc.scalar.activation(XZ_val[half][:, 0, j, :], XP[j % 2][:, 0:COLS], ACT.Identity,
                                     bias=bias[:, j:j + 1], scale=1.0 if j % G == 0 else 0.5).then_inc(xp_copied, 1)

            def copy_y(g):
                act.wait_ge(y_made, g + 1)
                if not (isinstance(g, int) and g == 0):
                    act.wait_ge(y_out, 16 * g)
                nc.scalar.activation(y_rows[:, :], y_ps[:, 0:D], ACT.Copy).then_inc(y_copied, 1)

            act.wait_ge(h0_T, 1)
            nc.scalar.activation(H0[:, 0:C * N], y_ps[:, 0:C * N], ACT.Copy, scale=2.0).then_inc(h0_copied, 1)
            copy_xT(0, 0)
            act.wait_ge(bias_made, 2)
            for j in range(TILES):
                copy_xp(0, 0, j)

            def step(t, s):
                par = s % 2
                for c in range(C):
                    act.wait_ge(summed[c], t + 1)
                    nc.scalar.activation(X[par][c][:, 1:1 + G, :].rearrange("q g n -> q (g n)"),
                                         Z[par][c][:, PARTS * G * N:(PARTS + 1) * G * N],
                                         ACT.Tanh).then_inc(gates_done[c], 1)
                for c in range(C):
                    act.wait_ge(S_done[c], t + 2)
                    nc.scalar.activation(tanh_c[c][:, :], X[1 - par][c][:, 0, :], ACT.Tanh,
                                         scale=0.5).then_inc(tanh_done[c], 1)

            def body(i, first, last):
                for half in range(HALVES):
                    g = i * HALVES + half
                    more = not (last and half == 1)
                    for s in range(TS):
                        step(i * STEPS + half * TS + s, s)
                        if s == 0 and more:
                            copy_xT(g + 1, 1 - half)
                        if s == 2 and not (first and half == 0):
                            copy_y(g - 1)
                        for j in range(TILES):
                            if more and proj_step(KD * j + KD - 1) + 1 == s:
                                copy_xp(g + 1, 1 - half, j)
            turns(act, body)
            copy_y(GROUPS - 1)

        @block.vector
        def _(dve):
            for c in range(C):
                nc.vector.memset(X[0][c][:, 0, :], 0.0).then_inc(S_done[c], 1)
            dve.wait_ge(consts_made, 3)
            nc.vector.tensor_copy(ident_bf[:, :], ident[:, :]).then_inc(ident_bf_made, 1)
            dve.wait_ge(bias_in, 16 * TILES)
            nc.vector.tensor_scalar(bias[:, :], bias_raw[:, :], 0.5, None, ALU.mult).then_inc(bias_made, 1)
            dve.wait_ge(bias_made, 1)
            nc.vector.tensor_copy(bias[:, 0:TILES:G], bias_raw[:, 0:TILES:G]).then_inc(bias_made, 1)
            dve.wait_ge(wh_in, 16)
            sig = slice(0, 3 * HID)
            tan = slice(3 * HID, 4 * HID)
            nc.vector.tensor_scalar(wh[:, :, sig], wh[:, :, sig], 0.25, None, ALU.mult).then_inc(wh_split, 1)
            nc.vector.tensor_scalar(wh[:, :, tan], wh[:, :, tan], 0.5, None, ALU.mult).then_inc(wh_split, 1)
            dve.wait_ge(wh_split, 2)
            nc.vector.tensor_copy(wh_part[0][:, :, :], wh[:, :, :]).then_inc(wh_split, 1)
            dve.wait_ge(wh_split, 3)
            nc.vector.tensor_tensor(wh_rest[:, :, :], wh[:, :, :], wh_part[0][:, :, :],
                                    ALU.subtract).then_inc(wh_split, 1)
            dve.wait_ge(wh_split, 4)
            nc.vector.tensor_copy(wh_part[1][:, :, :], wh_rest[:, :, :]).then_inc(wh_split, 1)
            dve.wait_ge(wh_split, 5)
            nc.vector.tensor_tensor(wh_part[2][:, :, :], wh_rest[:, :, :], wh_part[1][:, :, :],
                                    ALU.subtract).then_inc(wh_split, 1)
            dve.wait_ge(h0_copied, 1)
            for p in range(1, PARTS):
                if p > 1:
                    dve.wait_ge(H0_split, p - 1)
                nc.vector.tensor_tensor(H0_val[:, p, :, :], H0_val[:, p - 1, :, :], H0_up[:, p - 1, :, :, 1],
                                        ALU.subtract).then_inc(H0_split, 1)

            def add_parts(t, s, c):
                z = Z[s % 2][c]
                dve.wait_ge(z_done[c], t + 1)
                nc.vector.tensor_reduce(z[:, PARTS * G * N:(PARTS + 1) * G * N],
                                        z[:, 0:PARTS * G * N].rearrange("q (p m) -> q m p", p=PARTS),
                                        axis=AX.X, op=ALU.add).then_inc(summed[c], 1)

            def products(t, s, c):
                now = X[s % 2][c]
                dve.wait_ge(gates_done[c], t + 1)
                nc.vector.scalar_tensor_tensor(out=FI[c][:, :, :], in0=now[:, 2:4, :], scalar=1.0,
                                               in1=now[:, 0:2, :], op0=ALU.add, op1=ALU.mult).then_inc(fi_done[c], 1)

            def cell(t, s, c):
                dve.wait_ge(fi_done[c], t + 1)
                nc.vector.scalar_tensor_tensor(out=X[1 - s % 2][c][:, 0, :], in0=FI[c][:, 0, :], scalar=0.5,
                                               in1=FI[c][:, 1, :], op0=ALU.mult, op1=ALU.add).then_inc(S_done[c], 1)

            def state(t, half, s, c):
                dve.wait_ge(tanh_done[c], t + 1)
                nc.vector.scalar_tensor_tensor(out=H_val[half][:, c, 0, s, :], in0=X[s % 2][c][:, 4, :], scalar=1.0,
                                               in1=tanh_c[c][:, :], op0=ALU.add, op1=ALU.mult).then_inc(H_done[c], 1)

            def rest(t, half, s, c, p, before, after):
                dve.wait_ge(before, t + 1)
                nc.vector.tensor_tensor(H_val[half][:, c, p + 1, s, :], H_val[half][:, c, p, s, :],
                                        H_up[half][:, c, p, s, :, 1], ALU.subtract).then_inc(after, 1)

            def step(t, half, s):
                add_parts(t, s, 0)
                products(t, s, 0)
                add_parts(t, s, 1)
                cell(t, s, 0)
                products(t, s, 1)
                state(t, half, s, 0)
                cell(t, s, 1)
                rest(t, half, s, 0, 0, H_done[0], rest_done[0])
                rest(t, half, s, 0, 1, rest_done[0], state_done[0])
                state(t, half, s, 1)
                rest(t, half, s, 1, 0, H_done[1], rest_done[1])
                rest(t, half, s, 1, 1, rest_done[1], state_done[1])

            def body(i, first, last):
                for half in range(HALVES):
                    if not first:
                        dve.wait_ge(half_done, (i * HALVES + half - 1) * PIECES)
                    for s in range(TS):
                        step(i * STEPS + half * TS + s, half, s)
            turns(dve, body)

        @block.tensor
        def _(pe):
            def transpose_x(g, half, i):
                pe.wait_ge(x_in[half], 16 * (i + 1))
                if not (isinstance(g, int) and g == 0):
                    pe.wait_ge(xT_copied, g)
                for k in range(KD):
                    last = nc.tensor.transpose(xT_ps[:, k * COLS:(k + 1) * COLS], x_rows[half][:, k * P:(k + 1) * P],
                                               ident[:, :])
                last.then_inc(xT_made, 1)

            def project(g, half, m):
                j, k = divmod(m, KD)
                if m == 0:
                    pe.wait_ge(xT_copied, g + 1)
                if k == 0 and not (isinstance(g, int) and g == 0 and j < 2):
                    pe.wait_ge(xp_copied, g * TILES + j - 1)
                mm = nc.tensor.matmul(XP[j % 2][:, 0:COLS], gate_w(wx, k, j % G, j // G), xT[half][:, k, :],
                                      start=k == 0, stop=k == KD - 1)
                if k == KD - 1:
                    mm.then_inc(xp_made, 1)

            def transpose_y(g):
                pe.wait_ge(yT_done, (g + 1) * PIECES)
                if not (isinstance(g, int) and g == 0):
                    pe.wait_ge(y_copied, g)
                for c in range(C):
                    last = nc.tensor.transpose(y_ps[:, c * P:(c + 1) * P], yT[:, c, :], ident[:, :])
                last.then_inc(y_made, 1)

            def open_step(g, half, s):
                if s == 0:
                    pe.wait_ge(xz_rest, (g + 1) * (TILES // 2) * (PARTS - 1))
                for c in range(C):
                    nc.tensor.matmul(Z[s % 2][c][:, 0:PARTS * G * N], ident_bf[:, :],
                                     XZ_up[half][:, :, c * G:(c + 1) * G, s * N:(s + 1) * N, 1],
                                     start=True, stop=False, skip_group_check=True)

            def recur(half, s, k, c, gates, moving, last_k):
                z = Z[s % 2][c][:, 0:PARTS * G * N].rearrange("q (p g n) -> q p g n", p=PARTS, g=G)
                for g in gates:
                    for part in wh_part:
                        mm = nc.tensor.matmul(z[:, :, g, :], gate_w(part, k, g, c), moving, start=False, stop=last_k,
                                              skip_group_check=True)
                if last_k:
                    mm.then_inc(z_done[c], 1)

            pe.wait_ge(consts_made, 3)
            pe.wait_ge(h0_in, 16)
            for c in range(C):
                mm = nc.tensor.transpose(y_ps[:, c * N:(c + 1) * N], h0_rows[:, c * P:(c + 1) * P], ident[0:N, 0:N])
            mm.then_inc(h0_T, 1)
            transpose_x(0, 0, 0)
            pe.wait_ge(wx_in, 16)
            for m in range(MMS):
                project(0, 0, m)
            pe.wait_ge(ident_bf_made, 1)
            open_step(0, 0, 0)
            pe.wait_ge(wh_split, 6)

            def body(i, first, last):
                for half in range(HALVES):
                    g = i * HALVES + half
                    more = not (last and half == 1)
                    for s in range(TS):
                        t = i * STEPS + half * TS + s
                        start = first and half == 0 and s == 0
                        if start:
                            moving = [H0_up[:, :, k, :, 1] for k in range(C)]
                        elif s == 0:
                            moving = [H_up[1 - half][:, k, :, TS - 1, :, 1] for k in range(C)]
                        else:
                            moving = [H_up[half][:, k, :, s - 1, :, 1] for k in range(C)]
                        if start:
                            pe.wait_ge(H0_split, PARTS - 1)
                        else:
                            pe.wait_ge(state_done[0], t)
                        recur(half, s, 0, 0, range(G), moving[0], False)
                        recur(half, s, 0, 1, range(EARLY), moving[0], False)
                        if not start:
                            pe.wait_ge(state_done[1], t)
                        recur(half, s, 1, 0, range(G), moving[1], True)
                        recur(half, s, 0, 1, range(EARLY, G), moving[0], False)
                        recur(half, s, 1, 1, range(G), moving[1], True)
                        if s < TS - 1:
                            open_step(g, half, s + 1)
                        elif more:
                            open_step(g + 1, 1 - half, 0)
                        if s == 0 and more:
                            transpose_x(g + 1, 1 - half, i + half)
                        if s == 1 and not (first and half == 0):
                            transpose_y(g - 1)
                        for m in range(MMS):
                            if more and proj_step(m) == s:
                                project(g + 1, 1 - half, m)

            turns(pe, body)
            transpose_y(GROUPS - 1)


_INS = ["x", "cond_1024", "L0_cond_Wx", "L0_cond_Wh", "L0_cond_b"]
_OUT = ((8, 512, 256), "float32")


def kernel(**inputs):
    import numpy as _np
    import concourse.bacc as _bacc
    from concourse import mybir as _mybir
    from concourse.bass_utils import run_bass_kernel_spmd as _run

    nc = _bacc.Bacc("TRN2", target_bir_lowering=False, num_devices=1)
    arrays, args = {}, []
    for name in _INS:
        a = _np.ascontiguousarray(inputs[name])
        arrays[f"in_{name}"] = a
        args.append(nc.dram_tensor(f"in_{name}", a.shape, _mybir.dt.from_np(a.dtype), kind="ExternalInput").ap())
    args.append(nc.dram_tensor("out_0", _OUT[0], _mybir.dt.from_np(_np.dtype(_OUT[1])), kind="ExternalOutput").ap())
    lstm_residual(nc, *args)
    r = _run(nc, [arrays], core_ids=[0])
    return r.results[0]["out_0"]
```

```python
import concourse.bass as bass
from concourse import mybir
from contextlib import ExitStack


def lstm_residual(nc, x, h0, Wx, Wh, b, out):
    fp32 = mybir.dt.float32
    bf16 = mybir.dt.bfloat16
    ALU = mybir.AluOpType
    ACT = mybir.ActivationFunctionType
    AX = mybir.AxisListType

    N, T, D = x.shape
    HID = h0.shape[1]
    P = 128
    KD = D // P
    C = HID // P
    G = 4
    REF_GATE = [3, 1, 0, 2]
    PARTS = 3
    TS = 16
    COLS = TS * N
    HALVES = 2
    STEPS = TS * HALVES
    TURNS = T // STEPS
    GROUPS = T // TS
    TILES = C * G
    PIECES = 2
    PS = TS // PIECES
    FIRST = G - 1
    LOADS = FIRST * PARTS
    EARLY = 4

    ctx = ExitStack()
    with ctx:
        def sb(name, shape, dt=fp32):
            return ctx.enter_context(nc.sbuf_tensor(name, shape, dt))

        def ps(name, shape, dt=fp32):
            return ctx.enter_context(nc.psum_tensor(name, shape, dt))

        def sem(name):
            return ctx.enter_context(nc.semaphore(name))

        wx = sb("wx", [P, KD, G * HID])
        wh = sb("wh", [P, C, G * HID])
        wh_rest = sb("wh_rest", [P, C, G * HID])
        wh_part = [sb(f"wh_part{p}", [P, C, G * HID], bf16) for p in range(PARTS)]
        bias_rows = sb("bias_rows", [TILES, P])
        bias = sb("bias", [P, TILES])
        ident = sb("ident", [P, P])
        ident_bf = sb("ident_bf", [P, P], bf16)
        x_rows = [sb(f"x_rows{h}", [COLS, D]) for h in range(HALVES)]
        xT = [sb(f"xT{h}", [P, KD, COLS]) for h in range(HALVES)]
        XZ = [sb(f"XZ{h}", [P, PARTS * TILES * COLS]) for h in range(HALVES)]
        h0_rows = sb("h0_rows", [N, HID])
        H = [sb(f"H{h}", [P, C * PARTS * COLS]) for h in range(HALVES)]
        H0 = sb("H_init", [P, C * PARTS * N])
        halves = sb("halves", [P, C, PS * N])
        h_half = [sb(f"h_half{p}", [P, C, PS * N]) for p in range(PIECES)]
        yT = sb("yT", [P, C, COLS])
        y_rows = sb("y_rows", [COLS, D])
        X = [[sb(f"X{p}{c}", [P, 1 + G, N]) for c in range(C)] for p in range(2)]
        table_out = sb("table_out", [P, N])
        FI = [sb(f"FI{c}", [P, 2, N]) for c in range(C)]

        o_sum = [sb(f"o_sum{c}", [P, N]) for c in range(C)]

        Z = [[ps(f"Z{p}{c}", [P, 512]) for c in range(C)] for p in range(2)]
        ZO = [ps(f"ZO{c}", [P, 512]) for c in range(C)]
        XP = ps("XP", [P, 512])
        T_ps = ps("T_ps", [P, 512])
        PROJ0_BANKS = [XP] + ZO
        ZCOLS = slice(0, PARTS * FIRST * N)
        WH_FACTORS = [(slice(0, 3 * HID), 0.25), (slice(3 * HID, 4 * HID), 0.5)]
        SUMS = slice(ZCOLS.stop, ZCOLS.stop + FIRST * N)
        TANH_C = slice(SUMS.stop, SUMS.stop + N)
        OCOLS = slice(0, PARTS * N)

        wx_in = sem("wx_in")
        wh_in = [sem(f"wh_in{k}") for k in range(C)]
        bias_in = sem("bias_in")
        h0_in = sem("h0_in")
        x_in = [sem(f"x_in{h}") for h in range(HALVES)]
        consts_made = sem("consts_made")
        ident_bf_made = sem("ident_bf_made")
        bias_T = sem("bias_T")
        bias_made = sem("bias_made")
        wh_cast = sem("wh_cast")
        wh_split = sem("wh_split")
        h0_T = sem("h0_T")
        h0_copied = sem("h0_copied")
        H0_split = sem("H0_split")
        xT_made = sem("xT_made")
        xT_copied = sem("xT_copied")
        xp_made = sem("xp_made")
        xp_copied = sem("xp_copied")
        xz_rest = sem("xz_rest")
        z_done = [sem(f"z_done{c}") for c in range(C)]
        o_done = [sem(f"o_done{c}") for c in range(C)]
        o_summed = [sem(f"o_summed{c}") for c in range(C)]
        summed = [sem(f"summed{c}") for c in range(C)]
        gates_done = [sem(f"gates_done{c}") for c in range(C)]
        fi_done = [sem(f"fi_done{c}") for c in range(C)]
        S_done = [sem(f"S_done{c}") for c in range(C)]
        tanh_done = [sem(f"tanh_done{c}") for c in range(C)]
        H_done = [sem(f"H_done{c}") for c in range(C)]
        rest_done = [sem(f"rest_done{c}") for c in range(C)]
        state_done = [sem(f"state_done{c}") for c in range(C)]
        half_done = sem("half_done")
        yT_done = sem("yT_done")
        y_made = sem("y_made")
        y_copied = sem("y_copied")
        y_out = sem("y_out")

        H_val = [t[:, :].rearrange("q (c p t n) -> q c p t n", c=C, p=PARTS, t=TS) for t in H]
        H_up = [t[:, :].bitcast(bf16).rearrange("q (c p t n u) -> q c p t n u", c=C, p=PARTS, t=TS, u=2) for t in H]
        H0_val = H0[:, :].rearrange("q (p c n) -> q p c n", c=C, p=PARTS)
        H0_up = H0[:, :].bitcast(bf16).rearrange("q (p c n u) -> q p c n u", c=C, p=PARTS, u=2)
        XZ_val = [t[:, :].rearrange("q (p j t) -> q p j t", p=PARTS, j=TILES) for t in XZ]
        XZ_up = [t[:, :].bitcast(bf16).rearrange("q (p j t u) -> q p j t u", p=PARTS, j=TILES, u=2) for t in XZ]

        def gate_w(w, k, g, c):
            at = REF_GATE[g] * HID + c * P
            return w[:, k, at:at + P]

        PROJ = [(2, 2), (3, 4), (5, 6), (7, 8), (9, 10), (11, 12), (13, 13), (14, 14)]
        FILL = ((360,) * 4, (400,) * 3, (400,) * 2)
        FILL_AT = SUMS.stop + N

        block = ctx.enter_context(nc.Block())

        def turns(eng, body):
            body(0, True, False)
            with eng.Fori(1, TURNS - 1) as i:
                body(i, False, False)
            body(TURNS - 1, False, True)

        @block.sync
        def _(sp):
            def load_x(i, half):
                t0 = i * STEPS + half * TS
                src = x[:, bass.ds(t0, TS), :].rearrange("n t d -> t n d")
                sp.dma_start(x_rows[half][:, :], src).then_inc(x_in[half], 16)

            def store_y(t0):
                dst = out[:, bass.ds(t0, TS), :].rearrange("n t d -> t n d")
                sp.dma_start(dst, y_rows[:, :]).then_inc(y_out, 16)

            sp.dma_start(h0_rows[:, :], h0).then_inc(h0_in, 16)
            load_x(0, 0)
            sp.dma_start(bias_rows[:, :], b.rearrange("(j p) -> j p", p=P)).then_inc(bias_in, 16)
            sp.dma_start(wx[:, :, :], Wx.rearrange("(k p) n -> p k n", p=P)).then_inc(wx_in, 16)
            for k in range(C):
                sp.dma_start(wh[:, k, :], Wh[k * P:(k + 1) * P, :]).then_inc(wh_in[k], 16)
            load_x(0, 1)

            def body(i, first, last):
                for half in range(HALVES):
                    g = i * HALVES + half
                    if not last:
                        sp.wait_ge(xT_made, g + 1)
                        load_x(i + 1, half)
                    if not (first and half == 0):
                        sp.wait_ge(y_copied, g)
                        store_y(i * STEPS + half * TS - TS)
            turns(sp, body)
            sp.wait_ge(y_copied, GROUPS)
            store_y(T - TS)
            sp.wait_ge(y_out, 16 * GROUPS)

        @block.gpsimd
        def _(pool):
            nc.gpsimd.memset(ident[:, :], 0.0).then_inc(consts_made, 1)
            nc.gpsimd.memset(halves[:, :, :], 0.5).then_inc(consts_made, 1)
            pool.wait_ge(consts_made, 2)
            nc.gpsimd.affine_select(out=ident[:, :], in_=ident[:, :], compare_op=ALU.not_equal, fill=1.0, base=0,
                                    pattern=[[-1, P]], channel_multiplier=1).then_inc(consts_made, 1)

            def split_xz(g, half, j0, j1):
                lot = j0 // (j1 - j0)
                lots = TILES // (j1 - j0)
                pool.wait_ge(xp_copied, g * TILES + j1)
                for p in range(1, PARTS):
                    if p > 1:
                        pool.wait_ge(xz_rest, (g * lots + lot) * (PARTS - 1) + p - 1)
                    nc.gpsimd.tensor_tensor(XZ_val[half][:, p, j0:j1, :], XZ_val[half][:, p - 1, j0:j1, :],
                                            XZ_up[half][:, p - 1, j0:j1, :, 1], ALU.subtract).then_inc(xz_rest, 1)

            def residual(g, half, piece):
                done = g * TS + (piece + 1) * PS
                for c in range(C):
                    pool.wait_ge(H_done[c], done)
                if not (isinstance(g, int) and g == 0):
                    pool.wait_ge(y_made, g)
                pool.wait_ge(xT_copied, g + 1)
                s0, s1 = piece * PS, (piece + 1) * PS
                nc.gpsimd.tensor_tensor(h_half[piece][:, :, :], H_val[half][:, :, 0, s0:s1, :].rearrange("q c t n -> q c (t n)"),
                                        halves[:, :, :], ALU.mult).then_inc(half_done, 1)
                pool.wait_ge(half_done, g * PIECES + piece + 1)
                nc.gpsimd.tensor_tensor(yT[:, :, s0 * N:s1 * N], h_half[piece][:, :, :], xT[half][:, :, s0 * N:s1 * N],
                                        ALU.add).then_inc(yT_done, 1)

            for j in range(0, TILES, 2):
                split_xz(0, 0, j, j + 2)

            def body(i, first, last):
                for half in range(HALVES):
                    g = i * HALVES + half
                    more = not (last and half == 1)
                    if not (first and half == 0):
                        residual(g - 1, 1 - half, 1)
                    for j in range(0, TILES // 2, 2):
                        if more:
                            split_xz(g + 1, 1 - half, j, j + 2)
                    residual(g, half, 0)
                    for j in range(TILES // 2, TILES, 2):
                        if more:
                            split_xz(g + 1, 1 - half, j, j + 2)
            turns(pool, body)
            residual(GROUPS - 1, 1, 1)

        @block.scalar
        def _(act):
            def copy_xT(g, half):
                act.wait_ge(xT_made, g + 1)
                if not isinstance(g, int) or g >= 2:
                    act.wait_ge(yT_done, (g - 1) * PIECES)
                nc.scalar.activation(xT[half][:, :, :].rearrange("p k c -> p (k c)"), T_ps[:, 0:KD * COLS],
                                     ACT.Copy).then_inc(xT_copied, 1)

            def copy_xp(g, half, j):
                act.wait_ge(xp_made, g * TILES + j + 1)
                bank = PROJ0_BANKS[j % len(PROJ0_BANKS)] if isinstance(g, int) and g == 0 else XP
                nc.scalar.activation(XZ_val[half][:, 0, j, :], bank[:, 0:COLS], ACT.Identity,
                                     bias=bias[:, j:j + 1], scale=1.0 if j % G == 0 else 0.5).then_inc(xp_copied, 1)

            def copy_y(g):
                act.wait_ge(y_made, g + 1)
                if not (isinstance(g, int) and g == 0):
                    act.wait_ge(y_out, 16 * g)
                nc.scalar.activation(y_rows[:, :], T_ps[:, 0:D], ACT.Copy).then_inc(y_copied, 1)

            act.wait_ge(S_done[0], 1)
            nc.scalar.activation(table_out[:, :], X[0][0][:, 0, :], ACT.Tanh)
            act.wait_ge(h0_T, 1)
            act.wait_ge(bias_T, 1)
            nc.scalar.activation(H0[:, 0:C * N], T_ps[:, 0:C * N], ACT.Copy, scale=2.0).then_inc(h0_copied, 1)
            for g in range(G):
                at = C * N + REF_GATE[g] * C
                nc.scalar.activation(bias[:, g:TILES:G], T_ps[:, at:at + C], ACT.Copy,
                                     scale=1.0 if g == 0 else 0.5).then_inc(bias_made, 1)
            copy_xT(0, 0)
            act.wait_ge(bias_made, G)

            def cast_first(k):
                act.wait_ge(wh_in[k], 16)
                for cols, factor in WH_FACTORS:
                    nc.scalar.activation(wh_part[0][:, k, cols], wh[:, k, cols], ACT.Copy,
                                         scale=factor).then_inc(wh_cast, 1)

            def cast_second(k):
                act.wait_ge(wh_split, 2 * (k + 1))
                nc.scalar.activation(wh_part[1][:, k, :], wh_rest[:, k, :], ACT.Copy).then_inc(wh_cast, 1)

            for j in range(TILES):
                copy_xp(0, 0, j)
                if j in (1, 3):
                    cast_first(j // 2)
                if j in (5, 6):
                    cast_second(j - 5)

            def step(t, s):
                par = s % 2
                for c in range(C):
                    act.wait_ge(summed[c], t + 1)
                    nc.scalar.activation(X[par][c][:, 1:G, :].rearrange("q g n -> q (g n)"),
                                         Z[par][c][:, SUMS],
                                         ACT.Tanh).then_inc(gates_done[c], 1)
                for c in range(C):
                    act.wait_ge(o_summed[c], t + 1)
                    nc.scalar.activation(X[par][c][:, G, :], o_sum[c][:, :], ACT.Tanh)
                    act.wait_ge(S_done[c], t + 2)
                    nc.scalar.activation(Z[par][c][:, TANH_C], X[1 - par][c][:, 0, :], ACT.Tanh,
                                         scale=0.5).then_inc(tanh_done[c], 1)

            def body(i, first, last):
                for half in range(HALVES):
                    g = i * HALVES + half
                    more = not (last and half == 1)
                    for s in range(TS):
                        step(i * STEPS + half * TS + s, s)
                        if s == 0 and more:
                            copy_xT(g + 1, 1 - half)
                        if s == 2 and not (first and half == 0):
                            copy_y(g - 1)
                        for j in range(TILES):
                            if more and s == PROJ[j][KD - 1]:
                                copy_xp(g + 1, 1 - half, j)
            turns(act, body)
            copy_y(GROUPS - 1)

        @block.vector
        def _(dve):
            for c in range(C):
                nc.vector.memset(X[0][c][:, 0, :], 0.0).then_inc(S_done[c], 1)
            dve.wait_ge(consts_made, 3)
            nc.vector.tensor_copy(ident_bf[:, :], ident[:, :]).then_inc(ident_bf_made, 1)
            dve.wait_ge(h0_copied, 1)
            for p in range(1, PARTS):
                if p > 1:
                    dve.wait_ge(H0_split, p - 1)
                nc.vector.tensor_tensor(H0_val[:, p, :, :], H0_val[:, p - 1, :, :], H0_up[:, p - 1, :, :, 1],
                                        ALU.subtract).then_inc(H0_split, 1)
            for k in range(C):
                for n, (cols, factor) in enumerate(WH_FACTORS):
                    dve.wait_ge(wh_cast, 2 * k + n + 1)
                    nc.vector.scalar_tensor_tensor(out=wh_rest[:, k, cols], in0=wh[:, k, cols], scalar=factor,
                                                   in1=wh_part[0][:, k, cols], op0=ALU.mult,
                                                   op1=ALU.subtract).then_inc(wh_split, 1)
            for k in range(C):
                dve.wait_ge(wh_cast, 2 * C + k + 1)
                nc.vector.tensor_tensor(wh_part[2][:, k, :], wh_rest[:, k, :], wh_part[1][:, k, :],
                                        ALU.subtract).then_inc(wh_split, 1)
            def add_parts(t, s, c):
                z = Z[s % 2][c]
                dve.wait_ge(z_done[c], t + 1)
                nc.vector.tensor_reduce(z[:, SUMS], z[:, ZCOLS].rearrange("q (p m) -> q m p", p=PARTS),
                                        axis=AX.X, op=ALU.add).then_inc(summed[c], 1)

            def add_o_parts(t, c):
                dve.wait_ge(o_done[c], t + 1)
                nc.vector.tensor_reduce(o_sum[c][:, :], ZO[c][:, OCOLS].rearrange("q (p m) -> q m p", p=PARTS),
                                        axis=AX.X, op=ALU.add).then_inc(o_summed[c], 1)

            def products(t, s, c):
                now = X[s % 2][c]
                dve.wait_ge(gates_done[c], t + 1)
                nc.vector.scalar_tensor_tensor(out=FI[c][:, :, :], in0=now[:, 2:4, :], scalar=1.0,
                                               in1=now[:, 0:2, :], op0=ALU.add, op1=ALU.mult).then_inc(fi_done[c], 1)

            def cell(t, s, c):
                dve.wait_ge(fi_done[c], t + 1)
                nc.vector.scalar_tensor_tensor(out=X[1 - s % 2][c][:, 0, :], in0=FI[c][:, 0, :], scalar=0.5,
                                               in1=FI[c][:, 1, :], op0=ALU.mult, op1=ALU.add).then_inc(S_done[c], 1)

            def state(t, half, s, c):
                dve.wait_ge(tanh_done[c], t + 1)
                nc.vector.scalar_tensor_tensor(out=H_val[half][:, c, 0, s, :], in0=X[s % 2][c][:, 4, :], scalar=1.0,
                                               in1=Z[s % 2][c][:, TANH_C], op0=ALU.add, op1=ALU.mult).then_inc(H_done[c], 1)

            def rest(t, half, s, c, p, before, after):
                dve.wait_ge(before, t + 1)
                nc.vector.tensor_tensor(H_val[half][:, c, p + 1, s, :], H_val[half][:, c, p, s, :],
                                        H_up[half][:, c, p, s, :, 1], ALU.subtract).then_inc(after, 1)

            def step(t, half, s):
                add_parts(t, s, 0)
                add_parts(t, s, 1)
                products(t, s, 0)
                add_o_parts(t, 0)
                cell(t, s, 0)
                products(t, s, 1)
                add_o_parts(t, 1)
                cell(t, s, 1)
                state(t, half, s, 0)
                rest(t, half, s, 0, 0, H_done[0], rest_done[0])
                state(t, half, s, 1)
                rest(t, half, s, 0, 1, rest_done[0], state_done[0])
                rest(t, half, s, 1, 0, H_done[1], rest_done[1])
                rest(t, half, s, 1, 1, rest_done[1], state_done[1])

            def body(i, first, last):
                for half in range(HALVES):
                    if not first:
                        dve.wait_ge(half_done, (i * HALVES + half - 1) * PIECES)
                    for s in range(TS):
                        step(i * STEPS + half * TS + s, half, s)
            turns(dve, body)

        @block.tensor
        def _(pe):
            def transpose_x(g, half, i):
                pe.wait_ge(x_in[half], 16 * (i + 1))
                if not (isinstance(g, int) and g == 0):
                    pe.wait_ge(xT_copied, g)
                    if not isinstance(g, int) or g > 2:
                        pe.wait_ge(y_copied, g - 2)
                for k in range(KD):
                    last = nc.tensor.transpose(T_ps[:, k * COLS:(k + 1) * COLS], x_rows[half][:, k * P:(k + 1) * P],
                                               ident[:, :])
                last.then_inc(xT_made, 1)

            def project(g, half, j, k):
                if j == 0 and k == 0:
                    pe.wait_ge(xT_copied, g + 1)
                if k == 0 and not (isinstance(g, int) and g == 0):
                    pe.wait_ge(xp_copied, g * TILES + j)
                elif k == 0 and j >= len(PROJ0_BANKS):
                    pe.wait_ge(xp_copied, j + 1 - len(PROJ0_BANKS))
                bank = PROJ0_BANKS[j % len(PROJ0_BANKS)] if isinstance(g, int) and g == 0 else XP
                mm = nc.tensor.matmul(bank[:, 0:COLS], gate_w(wx, k, j % G, j // G), xT[half][:, k, :],
                                      start=k == 0, stop=k == KD - 1)
                if k == KD - 1:
                    mm.then_inc(xp_made, 1)

            def transpose_y(g, with_x=True):
                pe.wait_ge(yT_done, (g + 1) * PIECES)
                if not (isinstance(g, int) and g == 0):
                    pe.wait_ge(y_copied, g)
                pe.wait_ge(xT_copied, g + 3 if with_x else GROUPS)
                for c in range(C):
                    last = nc.tensor.transpose(T_ps[:, c * P:(c + 1) * P], yT[:, c, :], ident[:, :])
                last.then_inc(y_made, 1)

            def fill(s, widths):
                for n, cols in enumerate(widths):
                    nc.tensor.matmul(Z[s % 2][n % C][:, FILL_AT:FILL_AT + cols], ident_bf[:, :],
                                     wh_part[0][:, 0, 0:cols], start=True, stop=True)

            def open_step(g, half, s):
                if s == 0:
                    pe.wait_ge(xz_rest, (g + 1) * (TILES // 2) * (PARTS - 1))
                for c in range(C):
                    nc.tensor.matmul(Z[s % 2][c][:, ZCOLS], ident_bf[:, :],
                                     XZ_up[half][:, :, c * G:c * G + FIRST, s * N:(s + 1) * N, 1],
                                     start=True, stop=False, skip_group_check=True)

            def open_o(t, half, s, any_before):
                for c in range(C):
                    if any_before:
                        pe.wait_ge(o_summed[c], t)
                    nc.tensor.matmul(ZO[c][:, OCOLS], ident_bf[:, :],
                                     XZ_up[half][:, :, c * G + FIRST, s * N:(s + 1) * N, 1],
                                     start=True, stop=False, skip_group_check=True)

            def recur(s, k, c, first, end, moving, last_k):
                z = Z[s % 2][c][:, ZCOLS].rearrange("q (p g n) -> q p g n", p=PARTS, g=FIRST)
                for n in range(first, end):
                    g, part = divmod(n, PARTS)
                    mm = nc.tensor.matmul(z[:, :, g, :], gate_w(wh_part[part], k, g, c), moving, start=False,
                                          stop=last_k, skip_group_check=True)
                if last_k:
                    mm.then_inc(z_done[c], 1)

            def recur_o(c, moving):
                z = ZO[c][:, OCOLS].rearrange("q (p n) -> q p n", p=PARTS)
                for k in range(C):
                    for part in wh_part:
                        mm = nc.tensor.matmul(z, gate_w(part, k, FIRST, c), moving[k], start=False,
                                              stop=k == C - 1, skip_group_check=True)
                mm.then_inc(o_done[c], 1)

            pe.wait_ge(consts_made, 3)
            pe.wait_ge(h0_in, 16)
            for c in range(C):
                mm = nc.tensor.transpose(T_ps[:, c * N:(c + 1) * N], h0_rows[:, c * P:(c + 1) * P], ident[0:N, 0:N])
            mm.then_inc(h0_T, 1)
            pe.wait_ge(bias_in, 16)
            nc.tensor.transpose(T_ps[:, C * N:C * N + TILES], bias_rows[:, :], ident[0:TILES, 0:TILES])\
              .then_inc(bias_T, 1)
            pe.wait_ge(bias_made, G)
            transpose_x(0, 0, 0)
            pe.wait_ge(wx_in, 16)
            for j in range(TILES):
                for k in range(KD):
                    project(0, 0, j, k)
            pe.wait_ge(ident_bf_made, 1)
            open_step(0, 0, 0)
            open_o(0, 0, 0, False)
            pe.wait_ge(wh_split, 3 * C)

            def body(i, first, last):
                for half in range(HALVES):
                    g = i * HALVES + half
                    more = not (last and half == 1)
                    for s in range(TS):
                        t = i * STEPS + half * TS + s
                        start = first and half == 0 and s == 0
                        if start:
                            moving = [H0_up[:, :, k, :, 1] for k in range(C)]
                        elif s == 0:
                            moving = [H_up[1 - half][:, k, :, TS - 1, :, 1] for k in range(C)]
                        else:
                            moving = [H_up[half][:, k, :, s - 1, :, 1] for k in range(C)]
                        if start:
                            pe.wait_ge(H0_split, PARTS - 1)
                        else:
                            pe.wait_ge(state_done[0], t)
                        recur(s, 0, 0, 0, LOADS, moving[0], False)
                        recur(s, 0, 1, 0, EARLY, moving[0], False)
                        if not start:
                            pe.wait_ge(state_done[1], t)
                        recur(s, 1, 0, 0, LOADS, moving[1], True)
                        recur(s, 0, 1, EARLY, LOADS, moving[0], False)
                        recur(s, 1, 1, 0, LOADS, moving[1], True)
                        for c in range(C):
                            recur_o(c, moving)
                        if s < TS - 1 or more:
                            fill(s + 1, FILL[sum(steps.count(s) for steps in PROJ)])
                        if s < TS - 1:
                            open_step(g, half, s + 1)
                        elif more:
                            open_step(g + 1, 1 - half, 0)
                        if s == 0 and more:
                            transpose_x(g + 1, 1 - half, i + half)
                        if s == 1 and not (first and half == 0):
                            transpose_y(g - 1, more)
                        for j in range(TILES):
                            for k in range(KD):
                                if more and s == PROJ[j][k]:
                                    project(g + 1, 1 - half, j, k)
                        if s < TS - 1:
                            open_o(t + 1, half, s + 1, True)
                        elif more:
                            open_o(t + 1, 1 - half, 0, True)

            turns(pe, body)
            transpose_y(GROUPS - 1, False)


_INS = ["x", "cond_1024", "L0_cond_Wx", "L0_cond_Wh", "L0_cond_b"]
_OUT = ((8, 512, 256), "float32")


def kernel(**inputs):
    import numpy as _np
    import concourse.bacc as _bacc
    from concourse import mybir as _mybir
    from concourse.bass_utils import run_bass_kernel_spmd as _run

    nc = _bacc.Bacc("TRN2", target_bir_lowering=False, num_devices=1)
    arrays, args = {}, []
    for name in _INS:
        a = _np.ascontiguousarray(inputs[name])
        arrays[f"in_{name}"] = a
        args.append(nc.dram_tensor(f"in_{name}", a.shape, _mybir.dt.from_np(a.dtype), kind="ExternalInput").ap())
    args.append(nc.dram_tensor("out_0", _OUT[0], _mybir.dt.from_np(_np.dtype(_OUT[1])), kind="ExternalOutput").ap())
    lstm_residual(nc, *args)
    r = _run(nc, [arrays], core_ids=[0])
    return r.results[0]["out_0"]
```
